# Optimizing a Trainium2 kernel written in Bass

```python
import numpy as np
import jax
import jax.numpy as jnp

def _softmax(x, axis=-1):
    return jax.nn.softmax(x, axis=axis)

def _gelu(x):
    return jax.nn.gelu(x, approximate=True)

def _silu(x):
    return jax.nn.silu(x)

def _sigmoid(x):
    return jax.nn.sigmoid(x)

def _layernorm(x, axis=-1, eps=1e-05):
    m = jnp.mean(x, axis=axis, keepdims=True)
    v = jnp.var(x, axis=axis, keepdims=True)
    return (x - m) / jnp.sqrt(v + eps)

def _scatter_add(tgt, idx, src, axis=0):
    return tgt.at[idx].add(src)

def _segment_sum(src, seg, n):
    return jax.ops.segment_sum(src, seg, n)
kernel_name = 'mk_dlrm_tower_d1_rec_r8_be10d7'

def setup_inputs(seed: int=0):
    np.random.seed(seed)
    _w = jnp.asarray

    def _rec_inputs():
        import jax
        import jax.numpy as jnp
        _tk = jax.random.key(seed)
        ids = jnp.stack([jax.random.randint(jax.random.fold_in(_tk, 200 + f), (2048,), 0, v, jnp.int32) for f, v in enumerate([125000, 1000, 12500, 12500, 12500, 12500, 12500, 12500, 12500, 1250, 12500, 12500, 1000, 1000, 1000, 1250, 1000, 1000, 1000, 1250, 1000, 1250, 1000, 1000, 1000, 1000])], axis=1)
        tbl_0 = 0.05 * jax.random.normal(jax.random.fold_in(_tk, 500 + 0), (125000, 128), jnp.float32)
        tbl_1 = 0.05 * jax.random.normal(jax.random.fold_in(_tk, 500 + 1), (1000, 128), jnp.float32)
        tbl_2 = 0.05 * jax.random.normal(jax.random.fold_in(_tk, 500 + 2), (12500, 128), jnp.float32)
        tbl_3 = 0.05 * jax.random.normal(jax.random.fold_in(_tk, 500 + 3), (12500, 128), jnp.float32)
        tbl_4 = 0.05 * jax.random.normal(jax.random.fold_in(_tk, 500 + 4), (12500, 128), jnp.float32)
        tbl_5 = 0.05 * jax.random.normal(jax.random.fold_in(_tk, 500 + 5), (12500, 128), jnp.float32)
        tbl_6 = 0.05 * jax.random.normal(jax.random.fold_in(_tk, 500 + 6), (12500, 128), jnp.float32)
        tbl_7 = 0.05 * jax.random.normal(jax.random.fold_in(_tk, 500 + 7), (12500, 128), jnp.float32)
        tbl_8 = 0.05 * jax.random.normal(jax.random.fold_in(_tk, 500 + 8), (12500, 128), jnp.float32)
        tbl_9 = 0.05 * jax.random.normal(jax.random.fold_in(_tk, 500 + 9), (1250, 128), jnp.float32)
        tbl_10 = 0.05 * jax.random.normal(jax.random.fold_in(_tk, 500 + 10), (12500, 128), jnp.float32)
        tbl_11 = 0.05 * jax.random.normal(jax.random.fold_in(_tk, 500 + 11), (12500, 128), jnp.float32)
        tbl_12 = 0.05 * jax.random.normal(jax.random.fold_in(_tk, 500 + 12), (1000, 128), jnp.float32)
        tbl_13 = 0.05 * jax.random.normal(jax.random.fold_in(_tk, 500 + 13), (1000, 128), jnp.float32)
        tbl_14 = 0.05 * jax.random.normal(jax.random.fold_in(_tk, 500 + 14), (1000, 128), jnp.float32)
        tbl_15 = 0.05 * jax.random.normal(jax.random.fold_in(_tk, 500 + 15), (1250, 128), jnp.float32)
        tbl_16 = 0.05 * jax.random.normal(jax.random.fold_in(_tk, 500 + 16), (1000, 128), jnp.float32)
        tbl_17 = 0.05 * jax.random.normal(jax.random.fold_in(_tk, 500 + 17), (1000, 128), jnp.float32)
        tbl_18 = 0.05 * jax.random.normal(jax.random.fold_in(_tk, 500 + 18), (1000, 128), jnp.float32)
        tbl_19 = 0.05 * jax.random.normal(jax.random.fold_in(_tk, 500 + 19), (1250, 128), jnp.float32)
        tbl_20 = 0.05 * jax.random.normal(jax.random.fold_in(_tk, 500 + 20), (1000, 128), jnp.float32)
        tbl_21 = 0.05 * jax.random.normal(jax.random.fold_in(_tk, 500 + 21), (1250, 128), jnp.float32)
        tbl_22 = 0.05 * jax.random.normal(jax.random.fold_in(_tk, 500 + 22), (1000, 128), jnp.float32)
        tbl_23 = 0.05 * jax.random.normal(jax.random.fold_in(_tk, 500 + 23), (1000, 128), jnp.float32)
        tbl_24 = 0.05 * jax.random.normal(jax.random.fold_in(_tk, 500 + 24), (1000, 128), jnp.float32)
        tbl_25 = 0.05 * jax.random.normal(jax.random.fold_in(_tk, 500 + 25), (1000, 128), jnp.float32)
        _rk = jax.random.fold_in(_tk, 7)
        r_dense_x = -0.000514642 + 1.00011 * jax.random.normal(jax.random.fold_in(_rk, 101), (2048, 128), jnp.float32)
        W_top1 = 0.0456912 * jax.random.normal(jax.random.fold_in(_tk, 801), (479, 512), jnp.float32)
        W_top2 = 0.0441942 * jax.random.normal(jax.random.fold_in(_tk, 802), (512, 256), jnp.float32)
        W_top3 = 0.0625 * jax.random.normal(jax.random.fold_in(_tk, 803), (256, 1), jnp.float32)
        b_top1 = jnp.zeros((512,), jnp.float32)
        b_top2 = jnp.zeros((256,), jnp.float32)
        return (r_dense_x, ids, tbl_0, tbl_1, tbl_2, tbl_3, tbl_4, tbl_5, tbl_6, tbl_7, tbl_8, tbl_9, tbl_10, tbl_11, tbl_12, tbl_13, tbl_14, tbl_15, tbl_16, tbl_17, tbl_18, tbl_19, tbl_20, tbl_21, tbl_22, tbl_23, tbl_24, tbl_25, W_top1, b_top1, W_top2, b_top2, W_top3)
    r_dense_x, ids, tbl_0, tbl_1, tbl_2, tbl_3, tbl_4, tbl_5, tbl_6, tbl_7, tbl_8, tbl_9, tbl_10, tbl_11, tbl_12, tbl_13, tbl_14, tbl_15, tbl_16, tbl_17, tbl_18, tbl_19, tbl_20, tbl_21, tbl_22, tbl_23, tbl_24, tbl_25, W_top1, b_top1, W_top2, b_top2, W_top3 = _rec_inputs()

    def _L0_rec_setup():
        import jax, jax.numpy as jnp
        import numpy as np
        F = 26
        D = 128
        B = 2048
        _TRIU_I, _TRIU_J = np.triu_indices(F + 1, k=1)
        _TRIU_I = jnp.asarray(_TRIU_I)
        _TRIU_J = jnp.asarray(_TRIU_J)
        key = jax.random.key(seed)
        k1, k2 = jax.random.split(key)
        sparse_x = jax.random.normal(k1, (B, F, D), dtype=jnp.float32)
        dense_x = jax.random.normal(k2, (B, D), dtype=jnp.float32)
        return {'sparse_x': sparse_x, 'dense_x': dense_x}
    _L0_rec_all = _L0_rec_setup()
    _L0_rec_in = {k: v for k, v in _L0_rec_all.items() if k in ()}
    del _L0_rec_all
    return {'r_dense_x': r_dense_x, 'ids': ids, 'tbl_0': tbl_0, 'tbl_1': tbl_1, 'tbl_2': tbl_2, 'tbl_3': tbl_3, 'tbl_4': tbl_4, 'tbl_5': tbl_5, 'tbl_6': tbl_6, 'tbl_7': tbl_7, 'tbl_8': tbl_8, 'tbl_9': tbl_9, 'tbl_10': tbl_10, 'tbl_11': tbl_11, 'tbl_12': tbl_12, 'tbl_13': tbl_13, 'tbl_14': tbl_14, 'tbl_15': tbl_15, 'tbl_16': tbl_16, 'tbl_17': tbl_17, 'tbl_18': tbl_18, 'tbl_19': tbl_19, 'tbl_20': tbl_20, 'tbl_21': tbl_21, 'tbl_22': tbl_22, 'tbl_23': tbl_23, 'tbl_24': tbl_24, 'tbl_25': tbl_25, 'W_top1': W_top1, 'b_top1': b_top1, 'W_top2': W_top2, 'b_top2': b_top2, 'W_top3': W_top3}

def reference(r_dense_x, ids, tbl_0, tbl_1, tbl_2, tbl_3, tbl_4, tbl_5, tbl_6, tbl_7, tbl_8, tbl_9, tbl_10, tbl_11, tbl_12, tbl_13, tbl_14, tbl_15, tbl_16, tbl_17, tbl_18, tbl_19, tbl_20, tbl_21, tbl_22, tbl_23, tbl_24, tbl_25, W_top1, b_top1, W_top2, b_top2, W_top3):
    import jax
    import jax.numpy as jnp

    def _L0_rec_ref(sparse_x, dense_x):
        import jax, jax.numpy as jnp
        import numpy as np
        F = 26
        D = 128
        B = 2048
        _TRIU_I, _TRIU_J = np.triu_indices(F + 1, k=1)
        _TRIU_I = jnp.asarray(_TRIU_I)
        _TRIU_J = jnp.asarray(_TRIU_J)
        combined = jnp.concatenate([sparse_x, dense_x[:, None, :]], axis=1)
        interact = jnp.einsum('bfd,bgd->bfg', combined, combined)
        return interact[:, _TRIU_I, _TRIU_J]
    e = jnp.stack([tbl_0[ids[:, 0]], tbl_1[ids[:, 1]], tbl_2[ids[:, 2]], tbl_3[ids[:, 3]], tbl_4[ids[:, 4]], tbl_5[ids[:, 5]], tbl_6[ids[:, 6]], tbl_7[ids[:, 7]], tbl_8[ids[:, 8]], tbl_9[ids[:, 9]], tbl_10[ids[:, 10]], tbl_11[ids[:, 11]], tbl_12[ids[:, 12]], tbl_13[ids[:, 13]], tbl_14[ids[:, 14]], tbl_15[ids[:, 15]], tbl_16[ids[:, 16]], tbl_17[ids[:, 17]], tbl_18[ids[:, 18]], tbl_19[ids[:, 19]], tbl_20[ids[:, 20]], tbl_21[ids[:, 21]], tbl_22[ids[:, 22]], tbl_23[ids[:, 23]], tbl_24[ids[:, 24]], tbl_25[ids[:, 25]]], axis=1)
    z = _L0_rec_ref(e, r_dense_x)
    z = z.reshape(z.shape[0], -1)
    h = jnp.concatenate([z, r_dense_x], axis=1)
    h = jnp.maximum(h @ W_top1 + b_top1, 0.0)
    h = jnp.maximum(h @ W_top2 + b_top2, 0.0)
    y = h @ W_top3
    return y

_drawn_inputs = setup_inputs


def setup_inputs(seed=0):
    import zlib

    import numpy as np

    out = dict(_drawn_inputs(seed))
    spreads = {'b_top1': (0.0, 0.1), 'b_top2': (0.0, 0.1)}
    factors = {}
    for name, (base, spread) in spreads.items():
        noise = np.random.default_rng([zlib.crc32(name.encode()), seed]).standard_normal(out[name].shape)
        drawn = base * np.exp(spread * noise) if base else spread * noise
        out[name] = jnp.asarray(drawn.astype(out[name].dtype))
    for name, factor in factors.items():
        out[name] = (out[name] * factor).astype(out[name].dtype)
    return out
```

```python
from contextlib import ExitStack

import concourse.bass as bass
from concourse import mybir

ALU = mybir.AluOpType
ACT = mybir.ActivationFunctionType
F32 = mybir.dt.float32
I32 = mybir.dt.int32

P = 128
SPARSE = 26
FEATS = SPARSE + 1
FPAD = 32
GCOLS = 28
D = 128
TILE = 128
TPI = 2
QUADS = TILE // 4
GROUPS = [range(g, min(g + 4, FEATS)) for g in range(0, FEATS, 4)]
NG = len(GROUPS)
STEPS = 4
QPS = QUADS // STEPS


def pair_blocks():
    return [
        (1, 0, 0, 16, 16, 11),
        (1, 0, 0, 8, 8, 8),
        (1, 0, 16, 8, 24, 3),
        (3, 8, 0, 4, 4, 4),
        (6, 4, 0, 2, 2, 2),
        (1, 0, 24, 2, 26, 1),
        (13, 2, 0, 1, 1, 1),
    ]


def pair_order():
    def row(f, g):
        return f * (FEATS - 1) - f * (f - 1) // 2 + g - f - 1
    return [row(f0 + n * step + r, g0 + n * step + c)
            for blocks, step, f0, rows, g0, cols in pair_blocks()
            for n in range(blocks) for r in range(rows) for c in range(cols)]


NPAIRS = FEATS * (FEATS - 1) // 2
KC = 4
ZPAD = (KC - 1) * P


def dlrm_tower(nc, dense_x, ids, tables, w1_pairs, w1_dense, b1, w2, b2, w3, out):
    B = dense_x.shape[0]
    ITERS = B // (TILE * TPI)
    NB = TILE * TPI
    H1 = w1_pairs.shape[1]
    H2 = w2.shape[1]
    O1, O2 = H1 // P, H2 // P

    with ExitStack() as ctx:
        def sb(name, shape, dt=F32):
            return ctx.enter_context(nc.sbuf_tensor(name, shape, dt))

        def sem(name):
            return ctx.enter_context(nc.semaphore(name))

        idx = [sb(f"idx{t}", [P, SPARSE], I32) for t in range(TPI)]
        emb = [sb(f"emb{t}", [P, FEATS, D]) for t in range(TPI)]
        embT = [sb(f"embT{t}", [P, QUADS, 4, FPAD]) for t in range(TPI)]
        denseT = sb("denseT", [P, NB])
        gram = [sb(f"gram{t}", [P, FEATS, QUADS]) for t in range(TPI)]
        gramT = [sb(f"gramT{t}", [P, FPAD, FPAD]) for t in range(TPI)]
        z = [sb(f"z{t}", [P, ZPAD]) for t in range(TPI)]
        zT = sb("zT", [P, KC - 1, NB])
        h1T = sb("h1T", [P, O1, NB])
        h2T = sb("h2T", [P, O2, NB])
        y_row = sb("y_row", [1, NB])
        w1_sb = sb("w1_sb", [P, KC, H1])
        w2_sb = sb("w2_sb", [P, O1, H2])
        w3_sb = sb("w3_sb", [P, O2])
        b1_sb = sb("b1_sb", [P, O1])
        b2_sb = sb("b2_sb", [P, O2])
        ident = sb("ident", [P, P])

        tp_ps = [ctx.enter_context(nc.psum_tensor(f"tp_ps{k}", [P, 4, P], F32)) for k in range(2)]
        gram_ps = [ctx.enter_context(nc.psum_tensor(f"gram_ps{k}", [P, 2, 512], F32)) for k in range(2)]
        mlp_ps = ctx.enter_context(nc.psum_tensor("mlp_ps", [P, 1024], F32))

        s_weights = sem("s_weights")
        s_zero = sem("s_zero")
        s_ident0 = sem("s_ident0")
        s_ident = sem("s_ident")
        s_ids = [sem(f"s_ids{t}") for t in range(TPI)]
        s_dense = [sem(f"s_dense{t}") for t in range(TPI)]
        s_gathered = [sem(f"s_gathered{t}") for t in range(TPI)]
        s_gathering = sem("s_gathering")
        s_tp = sem("s_tp")
        s_embT_dve = sem("s_embT_dve")
        s_embT_act = sem("s_embT_act")
        s_gram = sem("s_gram")
        s_gout_act = sem("s_gout_act")
        s_gout_dve = sem("s_gout_dve")
        s_gramT = sem("s_gramT")
        s_z = sem("s_z")
        s_zt = sem("s_zt")
        s_zT = sem("s_zT")
        s_h1 = sem("s_h1")
        s_h1T = sem("s_h1T")
        s_h2 = sem("s_h2")
        s_h2T = sem("s_h2T")
        s_y = sem("s_y")
        s_yrow = sem("s_yrow")
        s_stored = sem("s_stored")

        ids_t = ids.rearrange("(n p) f -> n p f", p=TILE)
        dense_t = dense_x.rearrange("(n p) d -> n p d", p=TILE)
        out_t = out.rearrange("(n a b) o -> n a (b o)", a=1, b=NB)

        TPN = TPI * NG
        EVEN = [(NG + 1) // 2, NG // 2]
        ODD = [NG // 2, (NG + 1) // 2]
        GSN = TPI * STEPS

        block = ctx.enter_context(nc.Block())

        @block.sync
        def _(sp):
            def load_ids(i, t):
                sp.dma_start(idx[t][:], ids_t[i * TPI + t]).then_inc(s_ids[t], 16)

            def load_dense(i, t):
                sp.dma_start(emb[t][:, SPARSE, :], dense_t[i * TPI + t]).then_inc(s_dense[t], 16)

            for t in range(TPI):
                load_ids(0, t)
                load_dense(0, t)
            sp.dma_start(w1_sb[:, 0:KC - 2, :],
                         w1_pairs[0:(KC - 2) * P].rearrange("(c p) n -> p c n", p=P)).then_inc(s_weights, 16)
            sp.wait_ge(s_zero, 1)
            sp.dma_start(w1_sb[0:NPAIRS - (KC - 2) * P, KC - 2, :], w1_pairs[(KC - 2) * P:NPAIRS]).then_inc(s_weights, 16)
            sp.dma_start(w1_sb[:, KC - 1, :], w1_dense).then_inc(s_weights, 16)
            sp.dma_start(w2_sb[:], w2.rearrange("(c p) n -> p c n", p=P)).then_inc(s_weights, 16)
            with nc.allow_non_contiguous_dma(reason="small vectors"):
                sp.dma_start(w3_sb[:], w3.rearrange("(c p) n -> p (c n)", p=P)).then_inc(s_weights, 16)
                sp.dma_start(b1_sb[:], b1.rearrange("(c p) -> p c", p=P)).then_inc(s_weights, 16)
                sp.dma_start(b2_sb[:], b2.rearrange("(c p) -> p c", p=P)).then_inc(s_weights, 16)

            def store(i):
                sp.wait_ge(s_yrow, i + 1)
                sp.dma_start(out_t[i], y_row[:]).then_inc(s_stored, 16)

            def refill(i, first):
                for t in range(TPI):
                    sp.wait_ge(s_gathered[t], i * (16 * SPARSE))
                    load_ids(i, t)
                    sp.wait_ge(s_tp, i * TPN + (NG * (t + 1) - TPN))
                    load_dense(i, t)
                if not first:
                    store(i - 2)

            refill(1, True)
            with sp.Fori(2, ITERS) as i:
                refill(i, False)
            store(ITERS - 2)
            store(ITERS - 1)
            sp.wait_ge(s_stored, 16 * ITERS)

        @block.gpsimd
        def _(pool):
            nc.gpsimd.memset(ident[:], 0.0).then_inc(s_ident0, 1)
            pool.wait_ge(s_ident0, 1)
            nc.gpsimd.affine_select(out=ident[:], in_=ident[:], compare_op=ALU.not_equal, fill=1.0, base=0,
                                    pattern=[[-1, P]], channel_multiplier=1).then_inc(s_ident, 1)

            def gathers(i, first):
                for t in range(TPI):
                    pool.wait_ge(s_ids[t], i * 16 + 16)
                    if not first:
                        pool.wait_ge(s_tp, i * TPN + (NG * (t + 1) - TPN))
                    pool.sem_inc(s_gathering, 1)
                    for f in range(SPARSE):
                        nc.gpsimd.indirect_dma_start(
                            out=emb[t][:, f, :], out_offset=None, in_=tables[f],
                            in_offset=bass.IndirectOffsetOnAxis(ap=idx[t][:, f:f + 1], axis=0),
                        ).then_inc(s_gathered[t], 16)

            gathers(0, True)
            with pool.Fori(1, ITERS) as i:
                gathers(i, False)

        @block.tensor
        def _(pe):
            pe.wait_ge(s_ident, 1)

            def transposes(i, t, first):
                pe.wait_ge(s_gathered[t], i * (16 * SPARSE) + 16 * SPARSE)
                pe.wait_ge(s_dense[t], i * 16 + 16)
                for g, feats in enumerate(GROUPS):
                    n = t * NG + g
                    if not (first and n < 2):
                        if n % 2 == 0:
                            pe.wait_ge(s_embT_dve, i * NG + n // 2)
                        else:
                            pe.wait_ge(s_embT_act, i * NG + n // 2)
                    for k, f in enumerate(feats):
                        mm = pe.transpose(tp_ps[n % 2][:, k, :], emb[t][:, f, :], ident[:])
                    mm.then_inc(s_tp, 1)

            def gram_step(i, t, m, first):
                if m == 0:
                    pe.wait_ge(s_embT_dve, i * NG + sum(EVEN[:t + 1]))
                    pe.wait_ge(s_embT_act, i * NG + sum(ODD[:t + 1]))
                n = t * STEPS + m
                if not (first and n < 2):
                    pe.wait_ge(s_gout_act, i * GSN + (n - 1))
                    pe.wait_ge(s_gout_dve, i * GSN + (n - 1))
                for k in range(QPS):
                    q = m * QPS + k
                    bank = gram_ps[n % 2][:, k // 4, (k % 4) * 4 * GCOLS:(k % 4 + 1) * 4 * GCOLS]
                    mm = pe.matmul(bank, embT[t][:, q, :, :].rearrange("d s f -> d (s f)"), embT[t][:, q, :, 0:GCOLS], start=True, stop=True)
                mm.then_inc(s_gram, 1)

            def pairs(i, t):
                pe.wait_ge(s_z, i * TPI + t + 1)
                if t > 0:
                    pe.wait_ge(s_zT, i * TPI + t)
                for c in range(KC - 1):
                    mm = pe.transpose(mlp_ps[:, c * P:(c + 1) * P], z[t][:, c * P:(c + 1) * P], ident[:])
                mm.then_inc(s_zt, 1)

            def layer1(i, half, first):
                if half == 0:
                    pe.wait_ge(s_zT, i * TPI + TPI)
                elif not first:
                    pe.wait_ge(s_yrow, i)
                for o in range(half * 2, half * 2 + 2):
                    for c in range(KC):
                        rhs = zT[:, c, :] if c < KC - 1 else denseT[:]
                        mm = pe.matmul(mlp_ps[:, o * NB:(o + 1) * NB], w1_sb[:, c, o * P:(o + 1) * P], rhs,
                                       start=(c == 0), stop=(c == KC - 1))
                mm.then_inc(s_h1, 1)

            def layer2(i):
                pe.wait_ge(s_h1T, i * 2 + 2)
                for o in range(O2):
                    for c in range(O1):
                        mm = pe.matmul(mlp_ps[:, o * NB:(o + 1) * NB], w2_sb[:, c, o * P:(o + 1) * P], h1T[:, c, :],
                                       start=(c == 0), stop=(c == O1 - 1))
                mm.then_inc(s_h2, 1)

            def layer3(i):
                pe.wait_ge(s_h2T, i + 1)
                for c in range(O2):
                    mm = pe.matmul(mlp_ps[0:1, 512:512 + NB], w3_sb[:, c:c + 1], h2T[:, c, :],
                                   start=(c == 0), stop=(c == O2 - 1))
                mm.then_inc(s_y, 1)

            def mlp(i, first=False):
                pairs(i, 0)
                pairs(i, 1)
                layer1(i, 0, first)
                layer1(i, 1, first)
                layer2(i)
                layer3(i)

            def features(i, first):
                for t in range(TPI):
                    transposes(i, t, first)
                    for m in range(STEPS):
                        gram_step(i, t, m, first)

            features(0, True)
            pe.wait_ge(s_weights, 16 * 7)
            mlp(0, True)
            features(1, False)
            with pe.Fori(2, ITERS) as i:
                mlp(i - 1)
                features(i, False)
            mlp(ITERS - 1)

        def take_group(engine, copy, done, dtick, i, t, g, first):
            n = t * NG + g
            engine.wait_ge(s_tp, i * TPN + n + 1)
            if g < 2 and not first:
                engine.wait_ge(s_gram, i * GSN + (STEPS * (t + 1) - GSN))
            feats = GROUPS[g]
            k = len(feats)
            last = copy(embT[t][:, :, :, feats[0]:feats[0] + k].rearrange("d q s f -> d f s q"),
                        tp_ps[n % 2][:, 0:k, :].rearrange("d f (s q) -> d f s q", s=4))
            if SPARSE in feats:
                if not first:
                    engine.wait_ge(s_h1, i * 2)
                last = copy(denseT[:, t * TILE:(t + 1) * TILE], tp_ps[n % 2][:, k - 1, :])
            last.then_inc(done, 1)

        def gram_view(t, s, m):
            return gram[t][32 * s:32 * s + FPAD, :, m * QPS:(m + 1) * QPS].rearrange("f g (h q) -> f h q g", h=2)

        def gram_block(n, s):
            return gram_ps[n % 2][32 * s:32 * s + FPAD, :, 0:16 * GCOLS].rearrange(
                "f h (q s g) -> f s h q g", s=4, g=GCOLS)[:, s, :, :, 0:FEATS]

        def block_view(m, blocks, step, f0, rows, g0, cols):
            flat = m.rearrange("p g f -> p (g f)")
            at = g0 * FPAD + f0
            if blocks == 1:
                v = m[:, g0:g0 + cols, f0:f0 + rows].rearrange("p (n g) f -> p n g f", n=1)
            else:
                v = flat[:, at:at + blocks * step * (FPAD + 1)].rearrange("p (n x) -> p n x", n=blocks)
                v = v[:, :, 0:cols * FPAD].rearrange("p n (g f) -> p n g f", f=FPAD)[:, :, :, 0:rows]
            return v.rearrange("p n g f -> p n f g")

        @block.scalar
        def _(act):
            def copy(o, x):
                return nc.scalar.activation(o, x, ACT.Copy)

            act.wait_ge(s_zero, 3)

            def gram_out(i, t, m, first):
                n = t * STEPS + m
                act.wait_ge(s_gram, i * GSN + n + 1)
                if m == 0 and not first:
                    act.wait_ge(s_gramT, i * TPI + (t + 1 - TPI))
                for s in (0, 1, 2):
                    last = copy(gram_view(t, s, m), gram_block(n, s))
                last.then_inc(s_gout_act, 1)

            def mlp(i, first=False):
                for half in range(2):
                    act.wait_ge(s_h1, i * 2 + half + 1)
                    for o in range(half * 2, half * 2 + 2):
                        last = nc.scalar.activation(h1T[:, o, :], mlp_ps[:, o * NB:(o + 1) * NB], ACT.Relu,
                                                    bias=b1_sb[:, o:o + 1])
                    last.then_inc(s_h1T, 1)
                act.wait_ge(s_h2, i + 1)
                for o in range(O2):
                    last = nc.scalar.activation(h2T[:, o, :], mlp_ps[:, o * NB:(o + 1) * NB], ACT.Relu,
                                                bias=b2_sb[:, o:o + 1])
                last.then_inc(s_h2T, 1)
                act.wait_ge(s_y, i + 1)
                if not first:
                    act.wait_ge(s_stored, i * 16)
                copy(y_row[:], mlp_ps[0:1, 512:512 + NB]).then_inc(s_yrow, 1)

            def features(i, first):
                for t in range(TPI):
                    for g in range(NG):
                        if (t * NG + g) % 2 == 1:
                            take_group(act, copy, s_embT_act, None, i, t, g, first)
                    for m in range(STEPS):
                        gram_out(i, t, m, first)

            features(0, True)
            act.wait_ge(s_weights, 16 * 7)
            mlp(0, True)
            features(1, False)
            with act.Fori(2, ITERS) as i:
                mlp(i - 1)
                features(i, False)
            mlp(ITERS - 1)

        @block.vector
        def _(dve):
            copy = nc.vector.tensor_copy
            nc.vector.memset(w1_sb[64:P, KC - 2, :], 0.0).then_inc(s_zero, 1)
            for t in range(TPI):
                nc.vector.memset(z[t][:, NPAIRS:ZPAD], 0.0)
                nc.vector.memset(embT[t][:, :, :, FEATS:FPAD], 0.0).then_inc(s_zero, 1)

            def gram_out(i, t, m, first):
                n = t * STEPS + m
                dve.wait_ge(s_gram, i * GSN + n + 1)
                copy(gram_view(t, 3, m), gram_block(n, 3)).then_inc(s_gout_dve, 1)

            def compress(i, t, first):
                dve.wait_ge(s_gout_act, i * GSN + STEPS * (t + 1))
                dve.wait_ge(s_gout_dve, i * GSN + STEPS * (t + 1))
                nc.vector.transpose(gramT[t][:, 0:FEATS, :].rearrange("p g f -> p (g f)"),
                                    gram[t].rearrange("p g q -> p (g q)")).then_inc(s_gramT, 1)
                dve.wait_ge(s_gramT, i * TPI + t + 1)
                if not first:
                    dve.wait_ge(s_zt, i * TPI + (t + 1 - TPI))
                at = 0
                for blocks, step, f0, rows, g0, cols in pair_blocks():
                    n = blocks * rows * cols
                    dst = z[t][:, at:at + n].rearrange("p (n r c) -> p n r c", n=blocks, r=rows)
                    last = copy(dst, block_view(gramT[t], blocks, step, f0, rows, g0, cols))
                    at += n
                last.then_inc(s_z, 1)

            def pairs_out(i, t, first):
                dve.wait_ge(s_zt, i * TPI + t + 1)
                if t == 0 and not first:
                    dve.wait_ge(s_h1, i * 2)
                copy(zT[:, :, t * TILE:(t + 1) * TILE],
                     mlp_ps[:, 0:(KC - 1) * P].rearrange("p (c b) -> p c b", c=KC - 1)).then_inc(s_zT, 1)

            def features(i, first):
                for t in range(TPI):
                    for g in range(NG):
                        if (t * NG + g) % 2 == 0:
                            take_group(dve, copy, s_embT_dve, None, i, t, g, first)
                    for m in range(STEPS):
                        gram_out(i, t, m, first)
                    compress(i, t, first)

            features(0, True)
            pairs_out(0, 0, True)
            pairs_out(0, 1, True)
            with dve.Fori(1, ITERS) as i:
                features(i, False)
                for t in range(TPI):
                    pairs_out(i, t, False)


def kernel(**inputs):
    import numpy as np
    import concourse.bacc as bacc
    from concourse.bass_utils import run_bass_kernel_spmd

    nc = bacc.Bacc("TRN2", target_bir_lowering=False, num_devices=1)
    w1 = np.asarray(inputs["W_top1"])
    arrays = {
        "dense_x": inputs["r_dense_x"], "ids": inputs["ids"],
        **{f"tbl_{f}": inputs[f"tbl_{f}"] for f in range(SPARSE)},
        "w1_pairs": w1[np.array(pair_order())], "w1_dense": w1[NPAIRS:],
        "b1": inputs["b_top1"], "w2": inputs["W_top2"], "b2": inputs["b_top2"], "w3": inputs["W_top3"],
    }
    arrays = {k: np.ascontiguousarray(v) for k, v in arrays.items()}
    ap = {k: nc.dram_tensor(k, v.shape, mybir.dt.from_np(v.dtype), kind="ExternalInput").ap()
          for k, v in arrays.items()}
    out = nc.dram_tensor("y", (arrays["ids"].shape[0], 1), F32, kind="ExternalOutput").ap()
    dlrm_tower(nc, ap["dense_x"], ap["ids"], [ap[f"tbl_{f}"] for f in range(SPARSE)],
               ap["w1_pairs"], ap["w1_dense"], ap["b1"], ap["w2"], ap["b2"], ap["w3"], out)
    r = run_bass_kernel_spmd(nc, [arrays], core_ids=[0])
    return r.results[0]["y"]
```

```python
from contextlib import ExitStack

import concourse.bass as bass
from concourse import mybir

ALU = mybir.AluOpType
ACT = mybir.ActivationFunctionType
F32 = mybir.dt.float32
F32R = mybir.dt.float32r
I32 = mybir.dt.int32

P = 128
SPARSE = 26
FEATS = SPARSE + 1
FPAD = 32
GCOLS = FEATS - 1
D = 128
TILE = 128
TPI = 2
NB = TILE * TPI
QUADS = TILE // 4
STEPS = 4
QPS = QUADS // STEPS
GSN = TPI * STEPS

PICKED = [1, 12, 13, 14, 16, 17, 18, 20]
GATHERED = [f for f in range(SPARSE) if f not in PICKED]
NP_, NGA = len(PICKED), len(GATHERED)
SLOTS = GATHERED + [SPARSE] + PICKED
ROWS, CHUNKS = 125, 8
OH_BUFS = 2

T_GROUPS = [range(g, min(g + 4, NGA + 1)) for g in range(0, NGA + 1, 4)]
NPP, NT = NP_ // 2, len(T_GROUPS)
NGROUPS = NPP + TPI * NT

ORDER = [
    ("pick", 0), ("turn", 0, 0), ("turn", 0, 1), ("pairs", 0), ("pick", 1), ("turn", 0, 2),
    ("pairs", 1), ("turn", 0, 3), ("turn", 0, 4), ("layer", 0), ("pick", 2), ("layer", 1), ("pick", 3),
    ("layer", 2), ("turn", 1, 0), ("turn", 1, 1), ("layer", 3), ("turn", 1, 2), ("turn", 1, 3), ("turn", 1, 4),
    *(("gram", 0, m) for m in range(STEPS)), *(("gram", 1, m) for m in range(STEPS)),
]
BANKED = [e for e in ORDER if e[0] in ("pick", "turn")]
assert NP_ % 2 == 0 and NGROUPS % 2 == 0 and len(BANKED) == NGROUPS


def steps(first):
    return [e for e in ORDER if not (first and e[0] in ("pairs", "layer"))]


def group(*what):
    return BANKED.index(what)


def turned(t):
    return group("turn", t, NT - 1) + 1


def pair_blocks():
    return [
        (1, 0, 0, 16, 16, 11),
        (1, 0, 0, 8, 8, 8),
        (1, 0, 16, 8, 24, 3),
        (3, 8, 0, 4, 4, 4),
        (6, 4, 0, 2, 2, 2),
        (1, 0, 24, 2, 26, 1),
        (13, 2, 0, 1, 1, 1),
    ]


def pair_order():
    def row(f, g):
        f, g = sorted((SLOTS[f], SLOTS[g]))
        return f * (FEATS - 1) - f * (f - 1) // 2 + g - f - 1
    return [row(f0 + n * step + r, g0 + n * step + c)
            for blocks, step, f0, rows, g0, cols in pair_blocks()
            for n in range(blocks) for r in range(rows) for c in range(cols)]


NPAIRS = FEATS * (FEATS - 1) // 2
KC = 4
ZPAD = (KC - 1) * P


def dlrm_tower(nc, dense_x, ids, picked_ids, tables, w1_pairs, w1_dense, b1, w2, b2, w3, out):
    B = dense_x.shape[0]
    ITERS = B // NB
    H1 = w1_pairs.shape[1]
    H2 = w2.shape[1]
    O1, O2 = H1 // P, H2 // P

    with ExitStack() as ctx:
        def sb(name, shape, dt=F32):
            return ctx.enter_context(nc.sbuf_tensor(name, shape, dt))

        def sem(name):
            return ctx.enter_context(nc.semaphore(name))

        idx = [sb(f"idx{t}", [P, SPARSE], I32) for t in range(TPI)]
        emb = [sb(f"emb{t}", [P, NGA + 1, D]) for t in range(TPI)]
        embT_all = sb("embT", [P, TPI, QUADS, 4, FPAD])
        embT = [embT_all[:, t] for t in range(TPI)]
        staged = embT_all.rearrange("p t q s f -> p (t q s f)")[0:ROWS, 0:NP_ * CHUNKS * D].rearrange(
            "p (k x) -> p k x", k=NP_)
        table_hi = sb("table_hi", [P, NP_, CHUNKS, D], F32R)
        table_lo = sb("table_lo", [P, NP_, CHUNKS, D], F32R)
        pids = sb("pids", [P, NP_, NB], I32)
        pidf = pids.bitcast(F32)
        onehot = [sb(f"onehot{k}", [P, CHUNKS, 2, NB], F32R) for k in range(OH_BUFS)]
        row_int = sb("row_int", [P, 1], I32)
        row0 = sb("row0", [P, 1])
        dense = [sb(f"dense{t}", [P, D]) for t in range(TPI)]
        gram = [sb(f"gram{t}", [P, GCOLS, QUADS]) for t in range(TPI)]
        gramT = sb("gramT", [P, FPAD, FPAD])
        z = [sb(f"z{t}", [P, ZPAD]) for t in range(TPI)]
        zT = sb("zT", [P, KC, NB])
        h1T = sb("h1T", [P, O1, NB])
        h2T = sb("h2T", [P, O2, NB])
        y_row = sb("y_row", [1, NB])
        w1_sb = sb("w1_sb", [P, KC, H1])
        w2_sb = sb("w2_sb", [P, O1, H2])
        w3_sb = sb("w3_sb", [P, O2])
        b1_sb = sb("b1_sb", [P, O1])
        b2_sb = sb("b2_sb", [P, O2])
        ident = sb("ident", [P, P])

        group_ps = [ctx.enter_context(nc.psum_tensor(f"group_ps{k}", [P, 512], F32)) for k in range(2)]
        gram_ps = [ctx.enter_context(nc.psum_tensor(f"gram_ps{k}", [P, 2, 512], F32)) for k in range(2)]
        mlp_ps = ctx.enter_context(nc.psum_tensor("mlp_ps", [P, 1024], F32))

        s_weights = sem("s_weights")
        s_zero = sem("s_zero")
        s_zpad = sem("s_zpad")
        s_ident0 = sem("s_ident0")
        s_ident = sem("s_ident")
        s_rows = sem("s_rows")
        s_row0 = sem("s_row0")
        s_staged = [sem(f"s_staged{k}") for k in range(NP_)]
        s_hi = sem("s_hi")
        s_lo = sem("s_lo")
        s_pids = sem("s_pids")
        s_pidf = sem("s_pidf")
        s_onehot = sem("s_onehot")
        s_ids = [sem(f"s_ids{t}") for t in range(TPI)]
        s_dense = [sem(f"s_dense{t}") for t in range(TPI)]
        s_dense1 = [sem(f"s_dense1{t}") for t in range(TPI)]
        s_gathered = [sem(f"s_gathered{t}") for t in range(TPI)]
        s_gathering = sem("s_gathering")
        s_group = sem("s_group")
        s_out = sem("s_out")
        s_gram = sem("s_gram")
        s_gout = sem("s_gout")
        s_gramT = sem("s_gramT")
        s_z = sem("s_z")
        s_zt = sem("s_zt")
        s_zT = sem("s_zT")
        s_h1 = sem("s_h1")
        s_h1T = sem("s_h1T")
        s_h2 = sem("s_h2")
        s_h2T = sem("s_h2T")
        s_y = sem("s_y")
        s_yrow = sem("s_yrow")
        s_stored = sem("s_stored")

        ids_t = ids.rearrange("(n p) f -> n p f", p=TILE)
        dense_t = dense_x.rearrange("(n p) d -> n p d", p=TILE)
        out_t = out.rearrange("(n a b) o -> n a (b o)", a=1, b=NB)
        WEIGHT_LOADS = 7

        block = ctx.enter_context(nc.Block())

        @block.sync
        def _(sp):
            def load_ids(i, t):
                sp.dma_start(idx[t][:], ids_t[i * TPI + t]).then_inc(s_ids[t], 16)

            def load_dense(i, t):
                sp.dma_start(emb[t][:, NGA, :], dense_t[i * TPI + t]).then_inc(s_dense[t], 16)

            def load_dense1(i, t):
                sp.dma_start(dense[t][:], dense_t[i * TPI + t]).then_inc(s_dense1[t], 16)

            def load_pids(i):
                sp.dma_start(pids[:], picked_ids[i].partition_broadcast(P)).then_inc(s_pids, 16)

            def store(i):
                sp.wait_ge(s_yrow, i + 1)
                sp.dma_start(out_t[i], y_row[:]).then_inc(s_stored, 16)

            load_ids(0, 0)
            load_ids(0, 1)
            load_pids(0)
            for k, f in enumerate(PICKED):
                rows = tables[f].rearrange("(p c) d -> p (c d)", c=CHUNKS)
                for p0, p1 in ((0, ROWS // 16 * 16), (ROWS // 16 * 16, ROWS)):
                    sp.dma_start(staged[p0:p1, k, :], rows[p0:p1]).then_inc(s_staged[k], 16)
            load_dense(0, 0)
            load_dense(0, 1)
            sp.dma_start(w1_sb[:, 0:KC - 2, :],
                         w1_pairs[0:(KC - 2) * P].rearrange("(c p) n -> p c n", p=P)).then_inc(s_weights, 16)
            sp.wait_ge(s_zero, 1)
            sp.dma_start(w1_sb[0:NPAIRS - (KC - 2) * P, KC - 2, :], w1_pairs[(KC - 2) * P:NPAIRS]).then_inc(s_weights, 16)
            sp.dma_start(w1_sb[:, KC - 1, :], w1_dense).then_inc(s_weights, 16)
            sp.dma_start(w2_sb[:], w2.rearrange("(c p) n -> p c n", p=P)).then_inc(s_weights, 16)
            with nc.allow_non_contiguous_dma(reason="small vectors"):
                sp.dma_start(w3_sb[:], w3.rearrange("(c p) n -> p (c n)", p=P)).then_inc(s_weights, 16)
                sp.dma_start(b1_sb[:], b1.rearrange("(c p) -> p c", p=P)).then_inc(s_weights, 16)
                sp.dma_start(b2_sb[:], b2.rearrange("(c p) -> p c", p=P)).then_inc(s_weights, 16)

            def refill(i, first):
                sp.wait_ge(s_onehot, i * NPP)
                load_pids(i)
                for t in range(TPI):
                    sp.wait_ge(s_gathered[t], i * (16 * NGA))
                    load_ids(i, t)
                    sp.wait_ge(s_group, i * NGROUPS + (turned(t) - NGROUPS))
                    load_dense(i, t)
                if not first:
                    for t in range(TPI):
                        sp.wait_ge(s_zt, i * TPI + (t + 1 - 2 * TPI))
                        load_dense1(i - 1, t)
                    store(i - 2)

            for t in range(TPI):
                load_dense1(0, t)
            refill(1, True)
            with sp.Fori(2, ITERS) as i:
                refill(i, False)
            for t in range(TPI):
                sp.wait_ge(s_zt, (ITERS - 2) * TPI + t + 1)
                load_dense1(ITERS - 1, t)
            store(ITERS - 2)
            store(ITERS - 1)
            sp.wait_ge(s_stored, 16 * ITERS)

        @block.gpsimd
        def _(pool):
            nc.gpsimd.iota(row_int[:], pattern=[[0, 1]], base=0, channel_multiplier=-CHUNKS).then_inc(s_rows, 1)
            nc.gpsimd.memset(ident[:], 0.0).then_inc(s_ident0, 1)
            pool.wait_ge(s_ident0, 1)
            nc.gpsimd.affine_select(out=ident[:], in_=ident[:], compare_op=ALU.not_equal, fill=1.0, base=0,
                                    pattern=[[-1, P]], channel_multiplier=1).then_inc(s_ident, 1)

            def gathers(i, first):
                for t in range(TPI):
                    pool.wait_ge(s_ids[t], i * 16 + 16)
                    if not first:
                        pool.wait_ge(s_group, i * NGROUPS + (turned(t) - NGROUPS))
                    pool.sem_inc(s_gathering, 1)
                    for n, f in enumerate(GATHERED):
                        nc.gpsimd.indirect_dma_start(
                            out=emb[t][:, n, :], out_offset=None, in_=tables[f],
                            in_offset=bass.IndirectOffsetOnAxis(ap=idx[t][:, f:f + 1], axis=0),
                        ).then_inc(s_gathered[t], 16)

            gathers(0, True)
            with pool.Fori(1, ITERS) as i:
                gathers(i, False)

        @block.tensor
        def _(pe):
            pe.wait_ge(s_ident, 1)

            def wait_bank(i, n, first):
                if not (first and n < 2):
                    pe.wait_ge(s_out, i * NGROUPS + (n - 1))

            def pick(i, k, first):
                n = group("pick", k)
                wait_bank(i, n, first)
                if first:
                    pe.wait_ge(s_lo, 2 * k + 2)
                pe.wait_ge(s_onehot, i * NPP + k + 1)
                for g in range(2):
                    for part in (table_hi, table_lo):
                        for c in range(CHUNKS):
                            mm = pe.matmul(group_ps[n % 2][:, g * NB:(g + 1) * NB], part[0:ROWS, 2 * k + g, c, :],
                                           onehot[k % OH_BUFS][0:ROWS, c, g, :],
                                           start=(part is table_hi and c == 0),
                                           stop=(part is table_lo and c == CHUNKS - 1))
                mm.then_inc(s_group, 1)

            def turn(i, t, g, first):
                n = group("turn", t, g)
                if g == 0:
                    pe.wait_ge(s_gathered[t], i * (16 * NGA) + 16 * NGA)
                    pe.wait_ge(s_dense[t], i * 16 + 16)
                wait_bank(i, n, first)
                for k, f in enumerate(T_GROUPS[g]):
                    mm = pe.transpose(group_ps[n % 2][:, k * P:(k + 1) * P], emb[t][:, f, :], ident[:])
                mm.then_inc(s_group, 1)

            def gram_step(i, t, m, first):
                if m == 0:
                    pe.wait_ge(s_out, i * NGROUPS + max(turned(t), group("pick", NPP - 1) + 1))
                n = t * STEPS + m
                if not (first and n < 2):
                    pe.wait_ge(s_gout, i * GSN + (n - 1))
                for k in range(QPS):
                    q = m * QPS + k
                    bank = gram_ps[n % 2][:, k // 4, (k % 4) * 4 * GCOLS:(k % 4 + 1) * 4 * GCOLS]
                    mm = pe.matmul(bank, embT[t][:, q, :, :].rearrange("d s f -> d (s f)"),
                                   embT[t][:, q, :, 1:1 + GCOLS], start=True, stop=True)
                mm.then_inc(s_gram, 1)

            def pairs(i, t):
                pe.wait_ge(s_z, i * TPI + t + 1)
                if t > 0:
                    pe.wait_ge(s_zT, i * TPI + t)
                pe.wait_ge(s_dense1[t], i * 16 + 16)
                for c in range(KC):
                    rows = z[t][:, c * P:(c + 1) * P] if c < KC - 1 else dense[t][:]
                    mm = pe.transpose(mlp_ps[:, c * P:(c + 1) * P], rows, ident[:])
                mm.then_inc(s_zt, 1)

            def layer1(i, half, first):
                if half == 0:
                    pe.wait_ge(s_zT, i * TPI + TPI)
                elif not first:
                    pe.wait_ge(s_yrow, i)
                for o in range(half * O1 // 2, (half + 1) * O1 // 2):
                    for c in range(KC):
                        mm = pe.matmul(mlp_ps[:, o * NB:(o + 1) * NB], w1_sb[:, c, o * P:(o + 1) * P], zT[:, c, :],
                                       start=(c == 0), stop=(c == KC - 1))
                mm.then_inc(s_h1, 1)

            def layer2(i):
                pe.wait_ge(s_h1T, i * 2 + 2)
                for o in range(O2):
                    for c in range(O1):
                        mm = pe.matmul(mlp_ps[:, o * NB:(o + 1) * NB], w2_sb[:, c, o * P:(o + 1) * P], h1T[:, c, :],
                                       start=(c == 0), stop=(c == O1 - 1))
                mm.then_inc(s_h2, 1)

            def layer3(i):
                pe.wait_ge(s_h2T, i + 1)
                for c in range(O2):
                    mm = pe.matmul(mlp_ps[0:1, 512:512 + NB], w3_sb[:, c:c + 1], h2T[:, c, :],
                                   start=(c == 0), stop=(c == O2 - 1))
                mm.then_inc(s_y, 1)

            def layer(i, step, first):
                if step < 2:
                    layer1(i, step, first)
                elif step == 2:
                    layer2(i)
                else:
                    layer3(i)

            def iteration(i, before, first_mlp=False):
                first = before is None
                for kind, *what in steps(first):
                    if kind == "pick":
                        pick(i, *what, first)
                    elif kind == "turn":
                        turn(i, *what, first)
                    elif kind == "gram":
                        gram_step(i, *what, first)
                    elif kind == "pairs":
                        pairs(before, *what)
                    else:
                        layer(before, *what, first_mlp)

            iteration(0, None)
            pe.wait_ge(s_zpad, TPI)
            pe.wait_ge(s_weights, 16 * WEIGHT_LOADS)
            iteration(1, 0, True)
            with pe.Fori(2, ITERS) as i:
                iteration(i, i - 1)
            for t in range(TPI):
                pairs(ITERS - 1, t)
            for step in range(4):
                layer(ITERS - 1, step, False)

        def gram_view(t, s, m):
            return gram[t][32 * s:32 * s + FPAD, :, m * QPS:(m + 1) * QPS].rearrange("f g (h q) -> f h q g", h=2)

        def gram_block(n, s):
            return gram_ps[n % 2][32 * s:32 * s + FPAD, :, 0:16 * GCOLS].rearrange(
                "f h (q s g) -> f s h q g", s=4, g=GCOLS)[:, s]

        @block.scalar
        def _(act):
            def copy(o, x):
                return nc.scalar.activation(o, x, ACT.Copy)

            def convert_ids(i):
                act.wait_ge(s_pids, i * 16 + 16)
                nc.scalar.activation(pidf[:], pids[:], ACT.Identity, bias=row0[:, 0:1]).then_inc(s_pidf, 1)

            act.wait_ge(s_row0, 1)
            convert_ids(0)
            for k in range(NP_):
                act.wait_ge(s_staged[k], 32)
                copy(table_hi[0:ROWS, k].rearrange("p c d -> p (c d)"), staged[:, k, :]).then_inc(s_hi, 1)
            act.wait_ge(s_zero, 1 + TPI)

            def take_picked(i, k, first):
                n = group("pick", k)
                act.wait_ge(s_group, i * NGROUPS + n + 1)
                if k == 0 and not first:
                    act.wait_ge(s_gram, i * GSN)
                slot = NGA + 1 + 2 * k
                src = group_ps[n % 2].rearrange("d (f t s q) -> d t f s q", f=2, t=TPI, s=4)
                for t in range(TPI):
                    last = copy(embT[t][:, :, :, slot:slot + 2].rearrange("d q s f -> d f s q"), src[:, t])
                last.then_inc(s_out, 1)

            def take_turned(i, t, g, first):
                n = group("turn", t, g)
                act.wait_ge(s_group, i * NGROUPS + n + 1)
                if g == 0 and not first:
                    act.wait_ge(s_gram, i * GSN + (STEPS * (t + 1) - GSN))
                slots = T_GROUPS[g]
                k = len(slots)
                last = copy(embT[t][:, :, :, slots[0]:slots[0] + k].rearrange("d q s f -> d f s q"),
                            group_ps[n % 2][:, 0:k * P].rearrange("d (f s q) -> d f s q", f=k, s=4))
                last.then_inc(s_out, 1)

            def take_gram(i, t, m, first):
                n = t * STEPS + m
                act.wait_ge(s_gram, i * GSN + n + 1)
                if m == 0 and not first:
                    act.wait_ge(s_gramT, i * TPI + (t + 1 - TPI))
                for s in range(4):
                    last = copy(gram_view(t, s, m), gram_block(n, s))
                last.then_inc(s_gout, 1)

            def hidden1(i, half):
                act.wait_ge(s_h1, i * 2 + half + 1)
                for o in range(half * O1 // 2, (half + 1) * O1 // 2):
                    last = nc.scalar.activation(h1T[:, o, :], mlp_ps[:, o * NB:(o + 1) * NB], ACT.Relu,
                                                bias=b1_sb[:, o:o + 1])
                last.then_inc(s_h1T, 1)

            def hidden2(i):
                act.wait_ge(s_h2, i + 1)
                for o in range(O2):
                    last = nc.scalar.activation(h2T[:, o, :], mlp_ps[:, o * NB:(o + 1) * NB], ACT.Relu,
                                                bias=b2_sb[:, o:o + 1])
                last.then_inc(s_h2T, 1)

            def y_out(i, first):
                act.wait_ge(s_y, i + 1)
                if not first:
                    act.wait_ge(s_stored, i * 16)
                copy(y_row[:], mlp_ps[0:1, 512:512 + NB]).then_inc(s_yrow, 1)

            def layer(i, step, first):
                if step < 2:
                    hidden1(i, step)
                elif step == 2:
                    hidden2(i)
                else:
                    y_out(i, first)

            def iteration(i, before, first_mlp=False, last=False):
                first = before is None
                for kind, *what in steps(first):
                    if kind == "pick":
                        take_picked(i, *what, first)
                    elif kind == "turn":
                        take_turned(i, *what, first)
                    elif kind == "gram":
                        if what == [0, 0] and not last:
                            convert_ids(i + 1)
                        take_gram(i, *what, first)
                    elif kind == "layer":
                        layer(before, *what, first_mlp)

            iteration(0, None)
            act.wait_ge(s_weights, 16 * WEIGHT_LOADS)
            iteration(1, 0, True)
            with act.Fori(2, ITERS - 1) as i:
                iteration(i, i - 1)
            iteration(ITERS - 1, ITERS - 2, last=True)
            for step in range(4):
                layer(ITERS - 1, step, False)

        def block_view(blocks, step, f0, rows, g0, cols):
            at = (g0 - 1) * FPAD + f0
            if blocks == 1:
                v = gramT[:, g0 - 1:g0 - 1 + cols, f0:f0 + rows].rearrange("p (n g) f -> p n g f", n=1)
            else:
                flat = gramT.rearrange("p g f -> p (g f)")
                v = flat[:, at:at + blocks * step * (FPAD + 1)].rearrange("p (n x) -> p n x", n=blocks)
                v = v[:, :, 0:cols * FPAD].rearrange("p n (g f) -> p n g f", f=FPAD)[:, :, :, 0:rows]
            return v.rearrange("p n g f -> p n f g")

        @block.vector
        def _(dve):
            copy = nc.vector.tensor_copy
            dve.wait_ge(s_rows, 1)
            copy(row0[:], row_int[:]).then_inc(s_row0, 1)
            nc.vector.memset(w1_sb[64:P, KC - 2, :], 0.0).then_inc(s_zero, 1)
            for t in range(TPI):
                nc.vector.memset(z[t][:, NPAIRS:ZPAD], 0.0).then_inc(s_zpad, 1)

            def one_hot(i, k, first):
                if k == 0:
                    dve.wait_ge(s_pidf, i + 1)
                if not (first and k < OH_BUFS):
                    n = (group("pick", k - OH_BUFS) if k >= OH_BUFS
                         else group("pick", k - OH_BUFS + NPP) - NGROUPS)
                    dve.wait_ge(s_group, i * NGROUPS + (n + 1))
                for c in range(CHUNKS):
                    last = nc.vector.tensor_scalar(
                        onehot[k % OH_BUFS][0:ROWS, c].rearrange("p g b -> p (g b)"),
                        pidf[0:ROWS, 2 * k:2 * k + 2, :].rearrange("p g b -> p (g b)"), float(c), None, ALU.is_equal)
                last.then_inc(s_onehot, 1)

            for k in range(OH_BUFS):
                one_hot(0, k, True)
            for k in range(NP_):
                dve.wait_ge(s_hi, k + 1)
                nc.vector.tensor_tensor(table_lo[0:ROWS, k].rearrange("p c d -> p (c d)"), staged[:, k, :],
                                        table_hi[0:ROWS, k].rearrange("p c d -> p (c d)"),
                                        ALU.subtract).then_inc(s_lo, 1)
            dve.wait_ge(s_lo, NP_)
            for t in range(TPI):
                nc.vector.memset(embT[t][:, :, :, FEATS:FPAD], 0.0).then_inc(s_zero, 1)

            def compress(i, t, first):
                dve.wait_ge(s_gout, i * GSN + STEPS * (t + 1))
                if not (first and t == 0):
                    dve.wait_ge(s_z, i * TPI + t)
                nc.vector.transpose(gramT[:, 0:GCOLS, :].rearrange("p g f -> p (g f)"),
                                    gram[t].rearrange("p g q -> p (g q)")).then_inc(s_gramT, 1)
                dve.wait_ge(s_gramT, i * TPI + t + 1)
                if not first:
                    dve.wait_ge(s_zt, i * TPI + (t + 1 - TPI))
                at = 0
                for blocks, step, f0, rows, g0, cols in pair_blocks():
                    n = blocks * rows * cols
                    last = copy(z[t][:, at:at + n].rearrange("p (n r c) -> p n r c", n=blocks, r=rows),
                                block_view(blocks, step, f0, rows, g0, cols))
                    at += n
                last.then_inc(s_z, 1)

            def pairs_out(i, t, first):
                dve.wait_ge(s_zt, i * TPI + t + 1)
                if t == 0 and not first:
                    dve.wait_ge(s_h1, i * 2)
                copy(zT[:, :, t * TILE:(t + 1) * TILE],
                     mlp_ps[:, 0:KC * P].rearrange("p (c b) -> p c b", c=KC)).then_inc(s_zT, 1)

            def iteration(i, before, first_mlp=False, last=False):
                first = before is None
                for kind, *what in steps(first):
                    if kind == "pick" and what[0] + OH_BUFS < NPP:
                        one_hot(i, what[0] + OH_BUFS, first)
                    elif kind == "pairs":
                        pairs_out(before, *what, first_mlp)
                    elif kind == "gram" and what[1] == STEPS - 1:
                        compress(i, what[0], first)
                        if what[0] == 0 and not last:
                            for k in range(OH_BUFS):
                                one_hot(i + 1, k, False)

            iteration(0, None)
            iteration(1, 0, True)
            with dve.Fori(2, ITERS - 1) as i:
                iteration(i, i - 1)
            iteration(ITERS - 1, ITERS - 2, last=True)
            for t in range(TPI):
                pairs_out(ITERS - 1, t, False)


def kernel(**inputs):
    import numpy as np
    import concourse.bacc as bacc
    from concourse.bass_utils import run_bass_kernel_spmd

    nc = bacc.Bacc("TRN2", target_bir_lowering=False, num_devices=1)
    w1 = np.asarray(inputs["W_top1"])
    arrays = {
        "dense_x": inputs["r_dense_x"], "ids": inputs["ids"],
        "picked_ids": np.asarray(inputs["ids"]).reshape(-1, NB, SPARSE)[:, :, PICKED].transpose(0, 2, 1),
        **{f"tbl_{f}": inputs[f"tbl_{f}"] for f in range(SPARSE)},
        "w1_pairs": w1[np.array(pair_order())], "w1_dense": w1[NPAIRS:],
        "b1": inputs["b_top1"], "w2": inputs["W_top2"], "b2": inputs["b_top2"], "w3": inputs["W_top3"],
    }
    arrays = {k: np.ascontiguousarray(v) for k, v in arrays.items()}
    ap = {k: nc.dram_tensor(k, v.shape, mybir.dt.from_np(v.dtype), kind="ExternalInput").ap()
          for k, v in arrays.items()}
    out = nc.dram_tensor("y", (arrays["ids"].shape[0], 1), F32, kind="ExternalOutput").ap()
    dlrm_tower(nc, ap["dense_x"], ap["ids"], ap["picked_ids"], [ap[f"tbl_{f}"] for f in range(SPARSE)],
               ap["w1_pairs"], ap["w1_dense"], ap["b1"], ap["w2"], ap["b2"], ap["w3"], out)
    r = run_bass_kernel_spmd(nc, [arrays], core_ids=[0])
    return r.results[0]["y"]
```

```python
from contextlib import ExitStack

import concourse.bass as bass
from concourse import mybir

ALU = mybir.AluOpType
ACT = mybir.ActivationFunctionType
F32 = mybir.dt.float32
F32R = mybir.dt.float32r
I32 = mybir.dt.int32

P = 128
SPARSE = 26
FEATS = SPARSE + 1
FPAD = 32
GSLOTS = FEATS + 1
GCOLS = 2 * GSLOTS - 2
LOW0 = GSLOTS - 1
D = 128
TILE = 128
TPI = 2
NB = TILE * TPI
QUADS = TILE // 4
STEPS = 8
QPS = QUADS // STEPS
GSN = TPI * STEPS

PICKED = [1, 12, 13, 14, 16, 17, 18, 20]
GATHERED = [f for f in range(SPARSE) if f not in PICKED]
NP_, NGA = len(PICKED), len(GATHERED)
SLOTS = GATHERED + [SPARSE] + PICKED
ROWS, CHUNKS = 125, 8
OH_BUFS = 2
HALF = len(PICKED) // 2

T_GROUPS = [range(g, min(g + 4, NGA)) for g in range(0, NGA, 4)]
NT = len(T_GROUPS)
NTURNS = TPI * NT
NGROUPS = NP_ + NTURNS
LATE = PICKED[-4:]
T_GROUPS.append(range(NGA + 1 + NP_ - len(LATE), NGA + 1 + NP_))

FIRST = [
    ("split", 0), ("split", 1), ("split", 2), ("split", 3), ("onehot", 2), ("pick", 0), ("split", 4), ("split", 5),
    ("onehot", 3), ("onehot", 4), ("split", 6), ("onehot", 5), ("ids", 1), ("pick", 1), ("pick", 2), ("pick", 3),
    ("pick", 4), ("onehot", 6), ("turn", 0, 0), ("turn", 0, 1), ("split", 7), ("turn", 0, 2), ("pick", 5), ("ids", 0),
    ("onehot", 7), ("pick", 6), ("dense", 0), ("turn", 0, 3), ("pick", 7), ("turn", 0, 4), ("gram", 0, 0),
    ("gram", 0, 1), ("onehot", 0), ("gram", 0, 2), ("gram", 0, 3), ("gram", 0, 4), ("onehot", 1), ("turn", 1, 0),
    ("turn", 1, 1), ("gram", 0, 5), ("turn", 1, 2), ("gram", 0, 6), ("turn", 1, 3), ("turn", 1, 4), ("gram", 0, 7),
    ("gram", 1, 0), ("gram", 1, 1), ("add", 0), ("gram", 1, 2), ("gram", 1, 3), ("gram", 1, 4), ("gram", 1, 5),
    ("gram", 1, 6), ("gram", 1, 7), ("pairs", 0),
]
ORDER = [
    ("onehot", 2), ("pick", 0), ("ids", 1), ("add", 1), ("pick", 1), ("turn", 0, 0), ("onehot", 3), ("pick", 2),
    ("pairs", 1), ("turn", 0, 1), ("turn", 0, 2), ("layer", 0), ("dense", 0), ("turn", 0, 3), ("onehot", 4),
    ("pick", 3), ("onehot", 5), ("turn", 0, 4), ("ids", 0), ("onehot", 6), ("layer", 1), ("onehot", 7), ("onehot", 0),
    ("pick", 4), ("pick", 5), ("pick", 6), ("pick", 7), ("turn", 1, 0), ("gram", 0, 0), ("gram", 0, 1),
    ("turn", 1, 1), ("turn", 1, 2), ("gram", 0, 2), ("gram", 0, 3), ("layer", 2), ("gram", 0, 4), ("gram", 0, 5),
    ("turn", 1, 3), ("turn", 1, 4), ("gram", 0, 6), ("gram", 0, 7), ("layer", 3), ("gram", 1, 0), ("gram", 1, 1),
    ("layer", 4), ("add", 0), ("gram", 1, 2), ("gram", 1, 3), ("layer", 5), ("onehot", 1), ("gram", 1, 4),
    ("gram", 1, 5), ("layer", 6), ("gram", 1, 6), ("gram", 1, 7), ("pairs", 0),
]
LAST = [
    ("pick", 0), ("add", 1), ("turn", 0, 0), ("pick", 1), ("pairs", 1), ("onehot", 2), ("turn", 0, 1), ("turn", 0, 2),
    ("layer", 0), ("turn", 0, 3), ("onehot", 3), ("turn", 0, 4), ("layer", 1), ("pick", 2), ("pick", 3), ("dense", 0),
    ("turn", 1, 0), ("layer", 2), ("turn", 1, 1), ("turn", 0, 5), ("layer", 3), ("gram", 0, 0), ("gram", 0, 1),
    ("turn", 1, 2), ("turn", 1, 3), ("gram", 0, 2), ("gram", 0, 3), ("layer", 4), ("gram", 0, 4), ("gram", 0, 5),
    ("turn", 1, 4), ("turn", 1, 5), ("gram", 0, 6), ("gram", 0, 7), ("layer", 5), ("gram", 1, 0), ("gram", 1, 1),
    ("layer", 6), ("add", 0), ("gram", 1, 2), ("gram", 1, 3), ("pairs", 0), ("gram", 1, 4), ("gram", 1, 5),
    ("early", 0), ("gram", 1, 6), ("gram", 1, 7), ("early", 1), ("early", 2), ("early", 3), ("early", 4),
    ("early", 5), ("early", 6),
]
GRAM_SHARES = [1, 2, 0, 2, 2, 2, 1, 1, 1, 2, 1, 0, 1, 2, 2, 2]
NSHARES = sum(map(bool, GRAM_SHARES))


def banked(order):
    return [e for e in order if e[0] in ("pick", "turn")]


def turns(order):
    return [e for e in order if e[0] == "turn"]


def group(order, *what):
    return banked(order).index(what)


def turned(order, t):
    return group(order, "turn", t, NT - 1) + 1


def complete(groups, t):
    return 1 + max(n for n, g in enumerate(groups) if g[0] == "pick" or g[1] == t)


for order in (FIRST, ORDER):
    assert len(banked(order)) == NGROUPS and NGROUPS % 2 == 0


def shares_until(n):
    return sum(map(bool, GRAM_SHARES[:n]))


def pair_blocks():
    return [
        (1, 0, 0, 16, 16, 11),
        (1, 0, 0, 8, 8, 8),
        (1, 0, 16, 8, 24, 3),
        (3, 8, 0, 4, 4, 4),
        (6, 4, 0, 2, 2, 2),
        (1, 0, 24, 2, 26, 1),
        (13, 2, 0, 1, 1, 1),
    ]


def pair_order():
    def row(f, g):
        f, g = sorted((SLOTS[f], SLOTS[g]))
        return f * (FEATS - 1) - f * (f - 1) // 2 + g - f - 1
    return [row(f0 + n * step + r, g0 + n * step + c)
            for blocks, step, f0, rows, g0, cols in pair_blocks()
            for n in range(blocks) for r in range(rows) for c in range(cols)]


NPAIRS = FEATS * (FEATS - 1) // 2
KC = 4
ZPAD = (KC - 1) * P


def dlrm_tower(nc, dense_x, ids, picked_ids, tables, w1_pairs, w1_dense, b1, w2, b2, w3, out):
    B = ids.shape[0]
    ITERS = B // NB
    H1 = w1_pairs.shape[1]
    H2 = w2.shape[1]
    O1, O2 = H1 // P, H2 // P

    with ExitStack() as ctx:
        def sb(name, shape, dt=F32):
            return ctx.enter_context(nc.sbuf_tensor(name, shape, dt))

        def sem(name):
            return ctx.enter_context(nc.semaphore(name))

        idx = [sb(f"idx{t}", [P, SPARSE], I32) for t in range(TPI)]
        emb = [sb(f"emb{t}", [P, NGA, D]) for t in range(TPI)]
        HIGH, LOW = 0, 1
        embT = sb("embT", [P, TPI, QUADS, 2, 4, FPAD], F32R)
        table_hi = sb("table_hi", [P, NP_, CHUNKS, D], F32R)
        table_lo = sb("table_lo", [P, NP_, CHUNKS, D], F32R)
        pids = sb("pids", [P, NP_, NB], I32)
        pidf = pids.bitcast(F32)
        onehot = [sb(f"onehot{k}", [P, CHUNKS, NB], F32R) for k in range(OH_BUFS)]
        row_int = sb("row_int", [P, 1], I32)
        row0 = sb("row0", [P, 1])
        feat = sb("feat", [P, NB])
        grams = sb("grams", [P, 2, GCOLS, FPAD])
        gram = grams[:, 0]
        gramT = grams[:, 1]
        z = sb("z", [P, ZPAD])
        zT = sb("zT", [P, KC, NB])
        h1T = sb("h1T", [P, O1, NB])
        h2T = zT[:, 0:O2, :]
        y_row = h1T[0:1, 0, :]
        w1_sb = sb("w1_sb", [P, KC, H1])
        w2_sb = sb("w2_sb", [P, O1, H2])
        small = sb("small", [P, O2 + O1 + O2])
        w3_sb, b1_sb, b2_sb = small[:, 0:O2], small[:, O2:O2 + O1], small[:, O2 + O1:O2 + O1 + O2]
        ident = sb("ident", [P, P])
        staged = [buf[0:ROWS, at:at + CHUNKS * D] for buf, size in (
            (grams.rearrange("p r x f -> p (r x f)"), 2 * GCOLS * FPAD), (zT.rearrange("p c b -> p (c b)"), KC * NB),
            (h1T.rearrange("p c b -> p (c b)"), O1 * NB), (w1_sb.rearrange("p c n -> p (c n)"), KC * H1),
            (w2_sb.rearrange("p c n -> p (c n)"), O1 * H2))
            for at in range(0, size - CHUNKS * D + 1, CHUNKS * D)][:NP_]
        assert len(staged) == NP_

        group_ps = [ctx.enter_context(nc.psum_tensor(f"group_ps{k}", [P, 512], F32)) for k in range(2)]
        gram_ps = [ctx.enter_context(nc.psum_tensor(f"gram_ps{k}", [P, 2, 512], F32)) for k in range(2)]
        mlp_ps = ctx.enter_context(nc.psum_tensor("mlp_ps", [P, 1024], F32))

        s_weights = sem("s_weights")
        s_zero = sem("s_zero")
        s_zpad = sem("s_zpad")
        s_pads = sem("s_pads")
        s_ident0 = sem("s_ident0")
        s_ident = sem("s_ident")
        s_rows = sem("s_rows")
        s_row0 = sem("s_row0")
        s_staged = [sem(f"s_staged{k}") for k in range(NP_)]
        s_hi = sem("s_hi")
        s_lo = sem("s_lo")
        s_pids = [sem(f"s_pids{h}") for h in range(2)]
        s_pidf = [sem(f"s_pidf{h}") for h in range(2)]
        s_onehot = sem("s_onehot")
        s_ids = [sem(f"s_ids{t}") for t in range(TPI)]
        s_feat = sem("s_feat")
        s_feat_high = sem("s_feat_high")
        s_feat_low = sem("s_feat_low")
        s_dense = sem("s_dense")
        s_gathered = [sem(f"s_gathered{t}") for t in range(TPI)]
        s_late = [sem(f"s_late{t}") for t in range(TPI)]
        s_gathering = sem("s_gathering")
        s_group = sem("s_group")
        s_out = sem("s_out")
        s_low = sem("s_low")
        s_gram = sem("s_gram")
        s_gout = sem("s_gout")
        s_gout_dve = sem("s_gout_dve")
        s_gramT = sem("s_gramT")
        s_sum = sem("s_sum")
        s_z = sem("s_z")
        s_zt = sem("s_zt")
        s_zT = sem("s_zT")
        s_h1 = sem("s_h1")
        s_h1T = sem("s_h1T")
        s_h2 = sem("s_h2")
        s_h2T = sem("s_h2T")
        s_y = sem("s_y")
        s_yrow = sem("s_yrow")
        s_stored = sem("s_stored")

        ids_t = ids.rearrange("(n p) f -> n p f", p=TILE)
        out_t = out.rearrange("(n a b) o -> n a (b o)", a=1, b=NB)
        WEIGHT_LOADS = 7

        def first_batch(j):
            return isinstance(j, int) and j == 0

        block = ctx.enter_context(nc.Block())

        @block.sync
        def _(sp):
            def load_ids(i, t):
                sp.dma_start(idx[t][:], ids_t[i * TPI + t]).then_inc(s_ids[t], 16)

            def load_feat(i):
                sp.dma_start(feat[:], dense_x[i]).then_inc(s_feat, 16)

            def load_dense(i):
                sp.dma_start(zT[:, KC - 1, :], dense_x[i]).then_inc(s_dense, 16)

            def load_pids(i, h):
                part = slice(h * HALF, (h + 1) * HALF)
                sp.dma_start(pids[:, part, :], picked_ids[i][part].partition_broadcast(P)).then_inc(s_pids[h], 16)

            def store(i, last=False):
                sp.wait_ge(s_yrow, i + (2 if last else 1))
                sp.dma_start(out_t[i], y_row[:]).then_inc(s_stored, 16)

            load_ids(0, 0)
            load_pids(0, 0)
            load_ids(0, 1)
            load_feat(0)
            load_pids(0, 1)
            for k, f in enumerate(PICKED):
                rows = tables[f].rearrange("(p c) d -> p (c d)", c=CHUNKS)
                for p0, p1 in ((0, ROWS // 16 * 16), (ROWS // 16 * 16, ROWS)):
                    sp.dma_start(staged[k][p0:p1, :], rows[p0:p1]).then_inc(s_staged[k], 16)
            def load_weights():
                sp.wait_ge(s_zero, 1)
                sp.dma_start(w1_sb[:, 0:KC - 2, :],
                             w1_pairs[0:(KC - 2) * P].rearrange("(c p) n -> p c n", p=P)).then_inc(s_weights, 16)
                sp.dma_start(w1_sb[0:NPAIRS - (KC - 2) * P, KC - 2, :], w1_pairs[(KC - 2) * P:NPAIRS]).then_inc(s_weights, 16)
                sp.dma_start(w1_sb[:, KC - 1, :], w1_dense).then_inc(s_weights, 16)
                sp.dma_start(w2_sb[:], w2.rearrange("(c p) n -> p c n", p=P)).then_inc(s_weights, 16)
                with nc.allow_non_contiguous_dma(reason="small vectors"):
                    sp.dma_start(w3_sb, w3.rearrange("(c p) n -> p (c n)", p=P)).then_inc(s_weights, 16)
                    sp.dma_start(b1_sb, b1.rearrange("(c p) -> p c", p=P)).then_inc(s_weights, 16)
                    sp.dma_start(b2_sb, b2.rearrange("(c p) -> p c", p=P)).then_inc(s_weights, 16)

            def alongside(i, first):
                sp.wait_ge(s_gathered[0], i * (16 * NGA) + 16 * NGA)
                load_ids(i + 1, 0)
                sp.wait_ge(s_onehot, i * NP_ + HALF)
                load_pids(i + 1, 0)
                sp.wait_ge(s_feat_low, i + 1)
                load_feat(i + 1)
                sp.wait_ge(s_gathered[1], i * (16 * NGA) + 16 * NGA)
                load_ids(i + 1, 1)
                if first:
                    load_weights()
                sp.wait_ge(s_onehot, i * NP_ + NP_)
                load_pids(i + 1, 1)
                if not first:
                    sp.wait_ge(s_h1, i * 2)
                load_dense(i)
                if not first:
                    store(i - 1)

            alongside(0, True)
            with sp.Fori(1, ITERS - 1) as i:
                alongside(i, False)
            sp.wait_ge(s_h1, (ITERS - 1) * 2)
            load_dense(ITERS - 1)
            store(ITERS - 2)
            store(ITERS - 1, last=True)
            sp.wait_ge(s_stored, 16 * ITERS)

        @block.gpsimd
        def _(pool):
            nc.gpsimd.iota(row_int[:], pattern=[[0, 1]], base=0, channel_multiplier=-CHUNKS).then_inc(s_rows, 1)
            nc.gpsimd.memset(ident[:], 0.0).then_inc(s_ident0, 1)
            pool.wait_ge(s_ident0, 1)
            nc.gpsimd.affine_select(out=ident[:], in_=ident[:], compare_op=ALU.not_equal, fill=1.0, base=0,
                                    pattern=[[-1, P]], channel_multiplier=1).then_inc(s_ident, 1)

            def gathers(i, prev):
                for t in range(TPI):
                    pool.wait_ge(s_ids[t], i * 16 + 16)
                    if prev:
                        pool.wait_ge(s_group, i * NGROUPS + (turned(prev, t) - NGROUPS))
                    pool.sem_inc(s_gathering, 1)
                    for n, f in enumerate(GATHERED):
                        nc.gpsimd.indirect_dma_start(
                            out=emb[t][:, n, :], out_offset=None, in_=tables[f],
                            in_offset=bass.IndirectOffsetOnAxis(ap=idx[t][:, f:f + 1], axis=0),
                        ).then_inc(s_gathered[t], 16)

            gathers(0, None)
            gathers(1, FIRST)
            with pool.Fori(2, ITERS) as i:
                gathers(i, ORDER)
            pool.wait_ge(s_group, (ITERS - 1) * NGROUPS + turned(LAST, 0))
            pool.sem_inc(s_gathering, 1)
            for t in range(TPI):
                for n, f in enumerate(LATE):
                    nc.gpsimd.indirect_dma_start(
                        out=emb[0][:, t * len(LATE) + n, :], out_offset=None, in_=tables[f],
                        in_offset=bass.IndirectOffsetOnAxis(ap=idx[t][:, f:f + 1], axis=0),
                    ).then_inc(s_late[t], 16)

        @block.tensor
        def _(pe):
            pe.wait_ge(s_ident, 1)

            def wait_bank(i, n, order, prev):
                if n < 2 and not prev:
                    return
                holder = order if n >= 2 else prev
                before = banked(holder)[n - 2]
                if before[0] == "turn":
                    pe.wait_ge(s_low, i * NTURNS + (turns(holder).index(before) + 1 - (NTURNS if n < 2 else 0)))
                else:
                    pe.wait_ge(s_out, i * NGROUPS + (n - 1))

            def pick(i, order, prev, k):
                n = group(order, "pick", k)
                wait_bank(i, n, order, prev)
                if not prev:
                    pe.wait_ge(s_lo, k + 1)
                pe.wait_ge(s_onehot, i * NP_ + k + 1)
                for r, part in enumerate((table_hi, table_lo)):
                    for c in range(CHUNKS):
                        mm = pe.matmul(group_ps[n % 2][:, r * NB:(r + 1) * NB], part[0:ROWS, k, c, :],
                                       onehot[k % OH_BUFS][0:ROWS, c, :], start=(c == 0), stop=(c == CHUNKS - 1))
                mm.then_inc(s_group, 1)

            def turn(i, order, prev, t, g):
                n = group(order, "turn", t, g)
                if g == 0:
                    pe.wait_ge(s_gathered[t], i * (16 * NGA) + 16 * NGA)
                if g == NT:
                    pe.wait_ge(s_late[t], 16 * len(LATE))
                wait_bank(i, n, order, prev)
                for k, f in enumerate(T_GROUPS[g]):
                    rows = emb[t][:, f, :] if g < NT else emb[0][:, t * len(LATE) + k, :]
                    mm = pe.transpose(group_ps[n % 2][:, k * P:(k + 1) * P], rows, ident[:])
                mm.then_inc(s_group, 1)

            def gram_step(i, order, prev, t, m):
                if m == 0:
                    pe.wait_ge(s_out, i * NGROUPS + complete(banked(order), t))
                    pe.wait_ge(s_low, i * NTURNS + complete(turns(order), t))
                    pe.wait_ge(s_feat_low, i + 1)
                    if not prev and t == 0:
                        pe.wait_ge(s_pads, 1)
                n = t * STEPS + m
                if prev or n >= 2:
                    pe.wait_ge(s_gout, i * GSN + (n - 1))
                    if GRAM_SHARES[(n - 2) % GSN]:
                        pe.wait_ge(s_gout_dve, i * NSHARES + (shares_until((n - 2) % GSN + 1) - (NSHARES if n < 2 else 0)))
                for k in range(QPS):
                    q = m * QPS + k
                    products = gram_ps[n % 2][:, k // 2, (k % 2) * 8 * GSLOTS:(k % 2 + 1) * 8 * GSLOTS]
                    mm = pe.matmul(products.rearrange("p (s r g) -> p r s g", s=4, r=2),
                                   embT[:, t, q, HIGH].rearrange("d s f -> d (s f)"),
                                   embT[:, t, q, :, :, 0:GSLOTS], start=True, stop=True)
                mm.then_inc(s_gram, 1)

            def pairs(i, t):
                pe.wait_ge(s_z, i * TPI + t + 1)
                if t > 0:
                    pe.wait_ge(s_zT, i * TPI + t)
                for c in range(KC - 1):
                    mm = pe.transpose(mlp_ps[:, c * P:(c + 1) * P], z[:, c * P:(c + 1) * P], ident[:])
                mm.then_inc(s_zt, 1)

            def layer1(j, o, a, b):
                if o == 0:
                    pe.wait_ge(s_zT, (ITERS - 1) * TPI + b // TILE if b - a < NB else j * TPI + TPI)
                    pe.wait_ge(s_dense, ITERS * 16 if b - a < NB else j * 16 + 16)
                if o == O1 // 2 and not first_batch(j):
                    pe.wait_ge(s_yrow, j)
                for c in range(KC):
                    mm = pe.matmul(mlp_ps[:, o * NB + a:o * NB + b], w1_sb[:, c, o * P:(o + 1) * P], zT[:, c, a:b],
                                   start=(c == 0), stop=(c == KC - 1))
                if o % (O1 // 2) == O1 // 2 - 1:
                    mm.then_inc(s_h1, 1)

            def layer2(j, o, a, b):
                if o == 0:
                    pe.wait_ge(s_h1T, j * 2 + 2)
                for c in range(O1):
                    mm = pe.matmul(mlp_ps[:, o * NB + a:o * NB + b], w2_sb[:, c, o * P:(o + 1) * P], h1T[:, c, a:b],
                                   start=(c == 0), stop=(c == O1 - 1))
                if o == O2 - 1:
                    mm.then_inc(s_h2, 1)

            def layer3(j, a, b):
                pe.wait_ge(s_h2T, j + 1)
                for c in range(O2):
                    mm = pe.matmul(mlp_ps[0:1, 512 + a:512 + b], w3_sb[:, c:c + 1], h2T[:, c, a:b],
                                   start=(c == 0), stop=(c == O2 - 1))
                mm.then_inc(s_y, 1)

            def layer(j, part, a=0, b=NB):
                if part < O1:
                    layer1(j, part, a, b)
                elif part < O1 + O2:
                    layer2(j, part - O1, a, b)
                else:
                    layer3(j, a, b)

            def iteration(i, order, prev, before):
                for kind, *what in order:
                    if kind == "pick":
                        pick(i, order, prev, *what)
                    elif kind == "turn":
                        turn(i, order, prev, *what)
                    elif kind == "gram":
                        gram_step(i, order, prev, *what)
                    elif kind == "pairs":
                        pairs(i if what == [0] else before, *what)
                    elif kind == "layer":
                        layer(before, *what)
                    elif kind == "early":
                        layer(i, *what, 0, TILE)

            pe.wait_ge(s_zpad, 1)
            iteration(0, FIRST, None, None)
            pe.wait_ge(s_weights, 16 * WEIGHT_LOADS)
            iteration(1, ORDER, FIRST, 0)
            with pe.Fori(2, ITERS - 1) as i:
                iteration(i, ORDER, ORDER, i - 1)
            iteration(ITERS - 1, LAST, ORDER, ITERS - 2)
            pairs(ITERS - 1, 1)
            for part in range(O1 + O2 + 1):
                layer(ITERS, part, TILE, NB)

        def gram_view(s, m):
            return gram[32 * s:32 * s + FPAD, :, m * QPS:(m + 1) * QPS].rearrange("f x (h q) -> f h q x", h=2)

        def gram_block(n, s):
            return gram_ps[n % 2][32 * s:32 * s + FPAD, :, 0:16 * GSLOTS].rearrange(
                "f h (q s x) -> f s h q x", s=4, x=2 * GSLOTS)[:, s, :, :, 1:1 + GCOLS]

        def turned_slots(t, g, part):
            slots = T_GROUPS[g]
            return embT[:, t, :, part, :, slots[0]:slots[-1] + 1].rearrange("d q s f -> d f s q")

        def feat_slot(part):
            return embT[:, :, :, part, :, NGA].rearrange("d t q s -> d t s q")

        feat_view = feat.rearrange("d (t s q) -> d t s q", t=TPI, s=4)

        def turned_group(order, t, g):
            k = len(T_GROUPS[g])
            return group_ps[group(order, "turn", t, g) % 2][:, 0:k * P].rearrange("d (f s q) -> d f s q", f=k, s=4)

        @block.scalar
        def _(act):
            def copy(o, x):
                return nc.scalar.activation(o, x, ACT.Copy)

            def convert_ids(i, h):
                act.wait_ge(s_pids[h], i * 16 + 16)
                part = slice(h * HALF, (h + 1) * HALF)
                nc.scalar.activation(pidf[:, part, :], pids[:, part, :], ACT.Identity,
                                     bias=row0[:, 0:1]).then_inc(s_pidf[h], 1)

            def split_table(k):
                act.wait_ge(s_staged[k], 32)
                copy(table_hi[0:ROWS, k].rearrange("p c d -> p (c d)"), staged[k]).then_inc(s_hi, 1)

            def take_picked(i, order, prev, k):
                n = group(order, "pick", k)
                act.wait_ge(s_group, i * NGROUPS + n + 1)
                if k == 0 and prev:
                    act.wait_ge(s_gram, i * GSN)
                copy(embT.rearrange("d t q r s f -> d r s (t q) f")[:, :, :, :, NGA + 1 + k],
                     group_ps[n % 2].rearrange("d (r s x) -> d r s x", r=2, s=4)).then_inc(s_out, 1)

            def take_dense(i, prev):
                act.wait_ge(s_feat, i * 16 + 16)
                if prev:
                    act.wait_ge(s_gram, i * GSN)
                copy(feat_slot(HIGH), feat_view).then_inc(s_feat_high, 1)

            def take_turned(i, order, prev, t, g):
                act.wait_ge(s_group, i * NGROUPS + group(order, "turn", t, g) + 1)
                if g == 0 and prev:
                    act.wait_ge(s_gram, i * GSN + (STEPS * (t + 1) - GSN))
                copy(turned_slots(t, g, HIGH), turned_group(order, t, g)).then_inc(s_out, 1)

            def take_gram(i, t, m):
                n = t * STEPS + m
                act.wait_ge(s_gram, i * GSN + n + 1)
                if m == 0 and not (first_batch(i) and t == 0):
                    act.wait_ge(s_gramT, i * TPI + t)
                elif m == 0:
                    act.wait_ge(s_zero, 1)
                for s in range(4 - GRAM_SHARES[n]):
                    last = copy(gram_view(s, m), gram_block(n, s))
                last.then_inc(s_gout, 1)

            def pairs_out(i, t):
                act.wait_ge(s_zt, i * TPI + t + 1)
                copy(zT[:, 0:KC - 1, t * TILE:(t + 1) * TILE],
                     mlp_ps[:, 0:ZPAD].rearrange("p (c b) -> p c b", c=KC - 1)).then_inc(s_zT, 1)

            def hidden1(j, half, a, b):
                act.wait_ge(s_h1, j * 2 + half + 1)
                if half == 0 and not first_batch(j) and a == 0:
                    act.wait_ge(s_stored, j * 16)
                for o in range(half * O1 // 2, (half + 1) * O1 // 2):
                    last = nc.scalar.activation(h1T[:, o, a:b], mlp_ps[:, o * NB + a:o * NB + b], ACT.Relu,
                                                bias=b1_sb[:, o:o + 1])
                last.then_inc(s_h1T, 1)

            def hidden2(j, a, b):
                act.wait_ge(s_h2, j + 1)
                for o in range(O2):
                    last = nc.scalar.activation(h2T[:, o, a:b], mlp_ps[:, o * NB + a:o * NB + b], ACT.Relu,
                                                bias=b2_sb[:, o:o + 1])
                last.then_inc(s_h2T, 1)

            def y_out(j, a, b):
                act.wait_ge(s_y, j + 1)
                copy(y_row[:, a:b], mlp_ps[0:1, 512 + a:512 + b]).then_inc(s_yrow, 1)

            def layer(j, part, a=0, b=NB):
                if part in (O1 // 2 - 1, O1 - 1):
                    hidden1(j, part // (O1 // 2), a, b)
                elif part == O1 + O2 - 1:
                    hidden2(j, a, b)
                elif part == O1 + O2:
                    y_out(j, a, b)

            def iteration(i, order, prev, before):
                for kind, *what in order:
                    if kind == "split":
                        split_table(*what)
                    elif kind == "pick":
                        take_picked(i, order, prev, *what)
                    elif kind == "turn":
                        take_turned(i, order, prev, *what)
                    elif kind == "dense":
                        take_dense(i, prev)
                    elif kind == "gram":
                        take_gram(i, *what)
                    elif kind == "layer":
                        layer(before, *what)
                    elif kind == "early":
                        layer(i, *what, 0, TILE)
                    elif kind == "pairs":
                        pairs_out(i if what == [0] else before, *what)
                    elif kind == "ids":
                        convert_ids(i if what == [1] else i + 1, *what)

            act.wait_ge(s_rows, 1)
            copy(row0[:], row_int[:]).then_inc(s_row0, 1)
            act.wait_ge(s_row0, 1)
            convert_ids(0, 0)
            iteration(0, FIRST, None, None)
            act.wait_ge(s_weights, 16 * WEIGHT_LOADS)
            iteration(1, ORDER, FIRST, 0)
            with act.Fori(2, ITERS - 1) as i:
                iteration(i, ORDER, ORDER, i - 1)
            iteration(ITERS - 1, LAST, ORDER, ITERS - 2)
            pairs_out(ITERS - 1, 1)
            for part in range(O1 + O2 + 1):
                layer(ITERS, part, TILE, NB)

        def pair_view(column0, f_in_rows, blocks, step, f0, rows, g0, cols):
            c0, r0 = (g0, f0) if f_in_rows else (f0, g0)
            nc_, nr = (cols, rows) if f_in_rows else (rows, cols)
            at = (column0 + c0) * FPAD + r0
            flat = gramT.rearrange("p x f -> p (x f)")
            if blocks == 1:
                v = gramT[:, column0 + c0:column0 + c0 + nc_, r0:r0 + nr].rearrange("p (n x) f -> p n x f", n=1)
            else:
                size = step * (FPAD + 1)
                whole = flat[:, at:at + (blocks - 1) * size]
                v = bass.AP(tensor=whole.tensor, offset=whole.offset,
                            ap=[list(whole.ap[0]), [size, blocks], [FPAD, nc_], [1, nr]])
            return v.rearrange("p n x f -> p n f x") if f_in_rows else v

        @block.vector
        def _(dve):
            copy = nc.vector.tensor_copy
            nc.vector.memset(z[:, NPAIRS:ZPAD], 0.0).then_inc(s_zpad, 1)

            def one_hot(i, k, order=None):
                if k % HALF == 0:
                    dve.wait_ge(s_pidf[k // HALF], i + 1)
                if order:
                    before = (k - OH_BUFS) % NP_
                    n = group(order, "pick", before) - (NGROUPS if k < OH_BUFS else 0)
                    dve.wait_ge(s_group, i * NGROUPS + (n + 1))
                for c in range(CHUNKS):
                    last = nc.vector.tensor_scalar(onehot[k % OH_BUFS][0:ROWS, c, :], pidf[0:ROWS, k, :],
                                                   float(c), None, ALU.is_equal)
                last.then_inc(s_onehot, 1)

            def low_table(k):
                dve.wait_ge(s_hi, k + 1)
                nc.vector.tensor_tensor(table_lo[0:ROWS, k].rearrange("p c d -> p (c d)"), staged[k],
                                        table_hi[0:ROWS, k].rearrange("p c d -> p (c d)"),
                                        ALU.subtract).then_inc(s_lo, 1)
                if k == NP_ - 1:
                    dve.wait_ge(s_lo, NP_)
                    nc.vector.memset(w1_sb[64:P, KC - 2, :], 0.0).then_inc(s_zero, 1)

            def low_part(i, order, t, g):
                dve.wait_ge(s_out, i * NGROUPS + group(order, "turn", t, g) + 1)
                nc.vector.tensor_tensor(turned_slots(t, g, LOW), turned_group(order, t, g), turned_slots(t, g, HIGH),
                                        ALU.subtract).then_inc(s_low, 1)

            dve.wait_ge(s_zpad, 1)
            zeros = z[:, NPAIRS:NPAIRS + FPAD - FEATS]
            zeros = bass.AP(tensor=zeros.tensor, offset=zeros.offset, ap=[
                list(zeros.ap[0]), [0, TPI * QUADS * 2 * 4], [1, FPAD - FEATS]])
            copy(embT.rearrange("d t q r s f -> d (t q r s) f")[:, :, FEATS:FPAD], zeros).then_inc(s_pads, 1)
            for k in range(OH_BUFS):
                one_hot(0, k)

            def take_gram_share(i, t, m):
                n = t * STEPS + m
                dve.wait_ge(s_gram, i * GSN + n + 1)
                if not any(GRAM_SHARES[t * STEPS:n]) and not (first_batch(i) and t == 0):
                    dve.wait_ge(s_gramT, i * TPI + t)
                for s in range(4 - GRAM_SHARES[n], 4):
                    last = copy(gram_view(s, m), gram_block(n, s))
                last.then_inc(s_gout_dve, 1)

            def turn_gram(i, t):
                dve.wait_ge(s_gout, i * GSN + STEPS * (t + 1))
                dve.wait_ge(s_gout_dve, i * NSHARES + shares_until(STEPS * (t + 1)))
                if not (first_batch(i) and t == 0):
                    dve.wait_ge(s_z, i * TPI + t)
                nc.vector.transpose(gramT.rearrange("p x f -> p (x f)"),
                                    gram.rearrange("p x q -> p (x q)")).then_inc(s_gramT, 1)

            def add_terms(i, t):
                dve.wait_ge(s_gramT, i * TPI + t + 1)
                if not (first_batch(i) and t == 0):
                    dve.wait_ge(s_zt, i * TPI + t)
                for term in range(2):
                    at = 0
                    for blocks, step, f0, rows, g0, cols in pair_blocks():
                        n = blocks * rows * cols
                        pair = z[:, at:at + n].rearrange("p (n r c) -> p n r c", n=blocks, r=rows)
                        rectangle = (blocks, step, f0, rows, g0, cols)
                        if term == 0:
                            last = nc.vector.tensor_tensor(pair, pair_view(-1, True, *rectangle),
                                                           pair_view(LOW0, True, *rectangle), ALU.add)
                        else:
                            last = nc.vector.tensor_tensor(pair, pair, pair_view(LOW0, False, *rectangle), ALU.add)
                        at += n
                    if term == 0:
                        last.then_inc(s_sum, 1)
                        dve.wait_ge(s_sum, i * TPI + t + 1)
                last.then_inc(s_z, 1)

            def iteration(i, order, before):
                for kind, *what in order:
                    if kind == "split":
                        low_table(*what)
                    elif kind == "onehot":
                        one_hot(i if what[0] >= OH_BUFS else i + 1, *what, order)
                    elif kind == "turn":
                        low_part(i, order, *what)
                    elif kind == "dense":
                        dve.wait_ge(s_feat_high, i + 1)
                        nc.vector.tensor_tensor(feat_slot(LOW), feat_view, feat_slot(HIGH), ALU.subtract).then_inc(s_feat_low, 1)
                    elif kind == "gram":
                        t, m = what
                        if GRAM_SHARES[t * STEPS + m]:
                            take_gram_share(i, t, m)
                        if m == STEPS - 1:
                            turn_gram(i, t)
                    elif kind == "add":
                        add_terms(i if what == [0] else before, *what)

            iteration(0, FIRST, None)
            with dve.Fori(1, ITERS - 1) as i:
                iteration(i, ORDER, i - 1)
            iteration(ITERS - 1, LAST, ITERS - 2)
            add_terms(ITERS - 1, 1)


def kernel(**inputs):
    import numpy as np
    import concourse.bacc as bacc
    from concourse.bass_utils import run_bass_kernel_spmd

    nc = bacc.Bacc("TRN2", target_bir_lowering=False, num_devices=1)
    w1 = np.asarray(inputs["W_top1"])
    arrays = {
        "dense_x": np.asarray(inputs["r_dense_x"]).reshape(-1, NB, D).transpose(0, 2, 1),
        "ids": inputs["ids"],
        "picked_ids": np.asarray(inputs["ids"]).reshape(-1, TPI, 4, QUADS, SPARSE)[..., PICKED].transpose(
            0, 4, 2, 1, 3).reshape(-1, NP_, NB),
        **{f"tbl_{f}": inputs[f"tbl_{f}"] for f in range(SPARSE)},
        "w1_pairs": w1[np.array(pair_order())], "w1_dense": w1[NPAIRS:],
        "b1": inputs["b_top1"], "w2": inputs["W_top2"], "b2": inputs["b_top2"], "w3": inputs["W_top3"],
    }
    arrays = {k: np.ascontiguousarray(v) for k, v in arrays.items()}
    ap = {k: nc.dram_tensor(k, v.shape, mybir.dt.from_np(v.dtype), kind="ExternalInput").ap()
          for k, v in arrays.items()}
    out = nc.dram_tensor("y", (arrays["ids"].shape[0], 1), F32, kind="ExternalOutput").ap()
    dlrm_tower(nc, ap["dense_x"], ap["ids"], ap["picked_ids"], [ap[f"tbl_{f}"] for f in range(SPARSE)],
               ap["w1_pairs"], ap["w1_dense"], ap["b1"], ap["w2"], ap["b2"], ap["w3"], out)
    r = run_bass_kernel_spmd(nc, [arrays], core_ids=[0])
    return r.results[0]["y"]
```
